# Optimizing a Trainium2 kernel written in Bass

```python
import numpy as np
import jax
import jax.numpy as jnp

def _softmax(x, axis=-1):
    return jax.nn.softmax(x, axis=axis)
def _gelu(x):
    return jax.nn.gelu(x, approximate=True)
def _silu(x):
    return jax.nn.silu(x)
def _sigmoid(x):
    return jax.nn.sigmoid(x)
def _layernorm(x, axis=-1, eps=1e-5):
    m = jnp.mean(x, axis=axis, keepdims=True)
    v = jnp.var(x, axis=axis, keepdims=True)
    return (x - m) / jnp.sqrt(v + eps)
def _scatter_add(tgt, idx, src, axis=0):
    return tgt.at[idx].add(src)
def _segment_sum(src, seg, n):
    return jax.ops.segment_sum(src, seg, n)

kernel_name = 'mk_conv_preact_d1_conv_nchw192_f483bb'

def setup_inputs(seed: int = 0):
    np.random.seed(seed)
    _w = jnp.asarray
    def _rec_inputs():
        import jax
        import jax.numpy as jnp
        _gk = jax.random.key(seed)
        x = -4.65e-05 + 0.9999 * jax.random.normal(jax.random.fold_in(_gk, 1), (16, 192, 128, 128), jnp.float32)
        return x
    x = _rec_inputs()
    def _L0_conv_setup():
        import jax, jax.numpy as jnp
        from jax import lax
        import numpy as np
        B, C, H, W = (16, 192, 128, 128)
        key = jax.random.key(seed)
        k1, k2, k3 = jax.random.split(key, 3)
        x = jax.random.normal(k1, (B, C, H, W), dtype=jnp.float32)
        fan_in = C
        bound = 1.0 / np.sqrt(fan_in)
        merge_w = jax.random.uniform(k2, (C, C, 1, 1), dtype=jnp.float32, minval=-bound, maxval=bound)
        merge_b = jax.random.uniform(k3, (C,), dtype=jnp.float32, minval=-bound, maxval=bound)
        return {'x': x, 'merge_w': merge_w, 'merge_b': merge_b}
    _L0_conv_all = _L0_conv_setup()
    _L0_conv_in = {k: v for k, v in _L0_conv_all.items() if k in ('merge_w', 'merge_b', )}
    del _L0_conv_all

    return {
        "x": x,
        "L0_conv_merge_w": _L0_conv_in["merge_w"],
        "L0_conv_merge_b": _L0_conv_in["merge_b"],
    }

def reference(x, L0_conv_merge_w, L0_conv_merge_b):
    import jax
    import jax.numpy as jnp
    def _L0_conv_ref(x, merge_w, merge_b):
        import jax, jax.numpy as jnp
        from jax import lax
        import numpy as np
        B, C, H, W = (16, 192, 128, 128)
        c = x.shape[1]
        dn = lax.conv_dimension_numbers(x.shape, (c, 1, 3, 3), ('NCHW', 'OIHW', 'NCHW'))
        lap = jnp.array([[0.0, -1.0, 0.0], [-1.0, 4.0, -1.0], [0.0, -1.0, 0.0]], dtype=x.dtype)
        lap_k = jnp.broadcast_to(lap.reshape(1, 1, 3, 3), (c, 1, 3, 3))
        edges = lax.conv_general_dilated(x, lap_k, window_strides=(1, 1), padding=((1, 1), (1, 1)), dimension_numbers=dn, feature_group_count=c)
        out = x + edges
        dn1 = lax.conv_dimension_numbers(out.shape, merge_w.shape, ('NCHW', 'OIHW', 'NCHW'))
        y = lax.conv_general_dilated(out, merge_w, window_strides=(1, 1), padding='VALID', dimension_numbers=dn1)
        return y + merge_b[None, :, None, None]

    def _gn(v, G=32, eps=1e-5):
        B_, C_, H_, W_ = v.shape
        g = v.reshape(B_, G, C_ // G, H_, W_)
        m = jnp.mean(g, axis=(2, 3, 4), keepdims=True)
        s = jnp.var(g, axis=(2, 3, 4), keepdims=True)
        return ((g - m) / jnp.sqrt(s + eps)).reshape(v.shape)

    def _ln_c(v, eps=1e-6):
        m = jnp.mean(v, axis=1, keepdims=True)
        s = jnp.var(v, axis=1, keepdims=True)
        return (v - m) / jnp.sqrt(s + eps)

    def _ln_t(v, eps=1e-5):
        m = jnp.mean(v, axis=-1, keepdims=True)
        s = jnp.var(v, axis=-1, keepdims=True)
        return (v - m) / jnp.sqrt(s + eps)

    def _to_tokens(v):
        B_, C_, H_, W_ = v.shape
        return v.reshape(B_, C_, H_ * W_).transpose(0, 2, 1)
    def _from_tokens(t, like):
        B_, C_, H_, W_ = like.shape
        return t.transpose(0, 2, 1).reshape(B_, C_, H_, W_)

    x = x + _L0_conv_ref(_gn(x), L0_conv_merge_w, L0_conv_merge_b)
    return x


_drawn_inputs = setup_inputs


def setup_inputs(seed=0):
    import zlib

    import numpy as np

    out = dict(_drawn_inputs(seed))
    spreads = {}
    factors = {'L0_conv_merge_b': 4.49}
    for name, (base, spread) in spreads.items():
        noise = np.random.default_rng([zlib.crc32(name.encode()), seed]).standard_normal(out[name].shape)
        drawn = base * np.exp(spread * noise) if base else spread * noise
        out[name] = jnp.asarray(drawn.astype(out[name].dtype))
    for name, factor in factors.items():
        out[name] = (out[name] * factor).astype(out[name].dtype)
    return out
```

```python
from contextlib import ExitStack

import numpy as np

import concourse.bass as bass
from concourse import mybir
from concourse.alu_op_type import AluOpType as ALU

F32 = mybir.dt.float32
U8 = mybir.dt.uint8
ACT = mybir.ActivationFunctionType
AX = mybir.AxisListType

B, C, H, W = 16, 192, 128, 128
GROUPS = 32
GROUP_CHANNELS = C // GROUPS
GN_EPS = 1e-5

P = 128
CA = 128
CB = C - CA
HALF = H // 2
STREAMS = 3
SLOT_ROWS = 16
ROWS = SLOT_ROWS + 2
STEPS = HALF // SLOT_ROWS
STREAM = ROWS * W
SLOT = STREAMS * STREAM
RING = 6
SUB_ROWS = 8
SUBS = HALF // SUB_ROWS
SUB = SUB_ROWS * W
TILE_ROWS = SUB_ROWS // 2
TILE = TILE_ROWS * W
QW = W + 1
WTS_A, WTS_BA, WTS_BB = C, CA, P
WTS = WTS_A + WTS_BA + WTS_BB
PREP = 5


def conv_preact_kernel(nc: bass.Bass, x, w_lhst, bias_cols, group_avg, identity, out):
    x_flat = x.rearrange("b c h w -> b c (h w)")
    out_flat = out.rearrange("b c h w -> b c (h w)")
    x_half = x.rearrange("b c (u h) w -> b c u (h w)", u=2)
    out_half = out.rearrange("b c (u h) w -> b c u (h w)", u=2)

    with ExitStack() as ctx:
        def sb(name, shape, dt=F32):
            return ctx.enter_context(nc.sbuf_tensor(name, shape, dt))

        def pb(name, shape):
            return ctx.enter_context(nc.psum_tensor(name, shape, F32))

        def sem(name):
            return ctx.enter_context(nc.semaphore(name))

        ring = sb("ring", [P, RING * SLOT])
        q = sb("q", [P, STREAMS, SUB_ROWS + 1, QW])
        z = sb("z", [P, 2, STREAMS, SUB])
        unused = sb("unused", [P, SUB], U8)
        w_raw = sb("w_raw", [P, WTS])
        wts = sb("wts", [P, WTS])
        gavg = sb("gavg", [P, 4, P])
        ident = sb("ident", [P, P])
        zeros = sb("zeros", [P, W])
        bias_raw = sb("bias_raw", [P, 2])
        bias = sb("bias", [P, 2])
        partials = sb("partials", [P, 2, STREAMS, SUBS])
        sums = sb("sums", [P, 2, 2])
        mean = sb("mean", [P, STREAMS])
        square_mean = sb("square_mean", [P, 2])
        var = sb("var", [P, 2])
        var_eps = sb("var_eps", [P, 2])
        std = sb("std", [P, 2])
        rstd0 = sb("rstd0", [P, 2])
        rstd_sq = sb("rstd_sq", [P, 2])
        newton = sb("newton", [P, 2])
        rstd = sb("rstd", [P, 2])

        m1 = pb("m1", [P, 2, 2, TILE])
        m2 = pb("m2", [P, 2, TILE])
        small = pb("small", [P, 512])
        group_stats = small[:, 0:4].rearrange("p (g s) -> p g s", g=2)
        bias_sums = small[:, 4:6]

        consts_loaded = sem("consts_loaded")
        zeros_ready = sem("zeros_ready")
        loaded = [sem(f"loaded{k}") for k in range(STEPS)]
        stored = sem("stored")
        partial_ready = sem("partial_ready")
        sums_ready = sem("sums_ready")
        group_stats_ready = sem("group_stats_ready")
        mean_ready = sem("mean_ready")
        prep_step = sem("prep_step")
        var_ready = sem("var_ready")
        std_ready = sem("std_ready")
        rstd_ready = sem("rstd_ready")
        top_pads_ready = sem("top_pads_ready")
        bottom_pads_ready = sem("bottom_pads_ready")
        weights_ready = sem("weights_ready")
        bias_sums_ready = sem("bias_sums_ready")
        bias_ready = sem("bias_ready")
        q_ready = sem("q_ready")
        s_ready = sem("s_ready")
        z_ready = sem("z_ready")
        m1_ready = [sem(f"m1_ready{h}") for h in range(2)]
        m2_ready = [sem(f"m2_ready{h}") for h in range(2)]
        m1_evacuated = [sem(f"m1_evacuated{h}") for h in range(2)]
        m2_evacuated = [sem(f"m2_evacuated{h}") for h in range(2)]

        def load_count(k):
            return 16 * (4 if k in (0, STEPS - 1) else 3)

        STATS = 2 * STREAMS * SUBS

        def slot(img, k, turn=0):
            base = ((img * STEPS + (k + turn)) % RING) * SLOT
            return ring[:, bass.ds(base, SLOT)].rearrange("p (t r c) -> p t r c", t=STREAMS, r=ROWS)

        def rows(img, s, first, count):
            r = 1 + (s * SUB_ROWS) % SLOT_ROWS + first
            return slot(img, s * SUB_ROWS // SLOT_ROWS)[:, :, r:r + count, :]

        def wait_past(engine, semaphore, count):
            if not isinstance(count, int) or count > 0:
                engine.wait_ge(semaphore, count)

        block = ctx.enter_context(nc.Block())

        @block.sync
        def _(sp):
            def load(img, k):
                dst = slot(img, k)
                r0 = k * SLOT_ROWS - 1
                top0 = 1 if k == 0 else 0
                bot1 = ROWS - 1 if k == STEPS - 1 else ROWS
                if 0 < k < STEPS - 1:
                    sp.dma_start(dst[:, 0:2, :, :].rearrange("p t r c -> p t (r c)"),
                                 x_half[img, 0:CA, :, r0 * W:(r0 + ROWS) * W]).then_inc(loaded[k], 16)
                else:
                    sp.dma_start(dst[:, 0, top0:ROWS, :].rearrange("p r c -> p (r c)"),
                                 x_flat[img, 0:CA, (r0 + top0) * W:(r0 + ROWS) * W]).then_inc(loaded[k], 16)
                    sp.dma_start(dst[:, 1, 0:bot1, :].rearrange("p r c -> p (r c)"),
                                 x_flat[img, 0:CA, (HALF + r0) * W:(HALF + r0 + bot1) * W]).then_inc(loaded[k], 16)
                sp.dma_start(dst[0:CB, 2, top0:ROWS, :].rearrange("p r c -> p (r c)"),
                             x_flat[img, CA:C, (r0 + top0) * W:(r0 + ROWS) * W]).then_inc(loaded[k], 16)
                sp.dma_start(dst[CB:P, 2, 0:bot1, :].rearrange("p r c -> p (r c)"),
                             x_flat[img, CA:C, (HALF + r0) * W:(HALF + r0 + bot1) * W]).then_inc(loaded[k], 16)

            def store(img, s, k=None):
                sp.wait_ge(m1_evacuated[1], img * SUBS + s + 1)
                sp.wait_ge(m2_evacuated[1], img * SUBS + s + 1)
                src = rows(img, s, 0, SUB_ROWS)
                a, b = s * SUB, (s + 1) * SUB
                sp.dma_start(out_half[img, 0:CA, :, a:b],
                             src[:, 0:2, :, :].rearrange("p t r c -> p t (r c)")).then_inc(stored, 16)
                if k is not None:
                    before = k + RING - STEPS
                    sp.wait_ge(loaded[before % STEPS], load_count(before % STEPS) * (img + before // STEPS + 1))
                sp.dma_start(out_half[img, CA:C, 0, a:b],
                             src[0:CB, 2, :, :].rearrange("p r c -> p (r c)")).then_inc(stored, 16)
                sp.dma_start(out_half[img, CA:C, 1, a:b],
                             src[CB:P, 2, :, :].rearrange("p r c -> p (r c)")).then_inc(stored, 16)

            def image(img, loads):
                for k in range(STEPS):
                    subs = SUBS // STEPS
                    for s in range(k * subs, (k + 1) * subs):
                        store(img, s, k if k in loads and s % subs == 0 else None)
                    if k in loads:
                        sp.wait_ge(stored, 48 * (img * SUBS + (k + 1) * subs))
                        ahead = k + RING
                        load(img + ahead // STEPS, ahead % STEPS)

            sp.dma_start(w_raw[:, :], w_lhst).then_inc(consts_loaded, 16)
            sp.dma_start(gavg[:, :, :], group_avg).then_inc(consts_loaded, 16)
            sp.dma_start(ident[:, :], identity).then_inc(consts_loaded, 16)
            sp.dma_start(bias_raw[:, :], bias_cols).then_inc(consts_loaded, 16)
            for t in range(RING):
                if t >= STEPS:
                    sp.wait_ge(loaded[t % STEPS], load_count(t % STEPS))
                load(t // STEPS, t % STEPS)
            image(0, range(STEPS))
            with sp.Fori(1, B - 2) as img:
                image(img, range(STEPS))
            image(B - 2, range(RING - STEPS))
            image(B - 1, ())
            sp.wait_ge(stored, 48 * B * SUBS)

        @block.gpsimd
        def _(pool):
            pool.memset(zeros[:, :], 0.0).then_inc(zeros_ready, 1)

        @block.scalar
        def _(act):
            def statistics(img, k, kinds):
                act.wait_ge(loaded[k], load_count(k) * (img + 1))
                if k == 0 and 0 in kinds:
                    wait_past(act, sums_ready, img)
                for kind in kinds:
                    for n in range(2 * STREAMS):
                        t, half = n // 2, n % 2
                        first = 1 + half * SUB_ROWS
                        wait_past(act, partial_ready, img * STATS + (2 * k + kind) * 2 * STREAMS + n)
                        act.activation(unused[:, :],
                                       slot(img, k, RING * kind)[:, t, first:first + SUB_ROWS, :].rearrange("p r c -> p (r c)"),
                                       ACT.Square if kind else ACT.Identity,
                                       accum_out=partials[:, kind, t, 2 * k + half:2 * k + half + 1]
                                       ).then_inc(partial_ready, 1)

            def pads_and_std(img):
                act.wait_ge(mean_ready, img + 1)
                top, bottom = slot(img, 0), slot(img, STEPS - 1)
                act.activation(top[:, 0, 0, :], zeros[:, :], ACT.Identity, bias=mean[:, 0:1])
                act.activation(top[0:CB, 2, 0, :], zeros[0:CB, :], ACT.Identity,
                               bias=mean[0:CB, 2:3]).then_inc(top_pads_ready, 1)
                act.wait_ge(var_ready, img + 1)
                act.activation(std[:, :], var_eps[:, :], ACT.Sqrt).then_inc(std_ready, 1)
                act.activation(bottom[:, 1, ROWS - 1, :], zeros[:, :], ACT.Identity, bias=mean[:, 1:2])
                act.activation(bottom[CB:P, 2, ROWS - 1, :], zeros[CB:P, :], ACT.Identity,
                               bias=mean[CB:P, 2:3]).then_inc(bottom_pads_ready, 1)

            def scale_weights(img):
                act.wait_ge(rstd_ready, img + 1)
                wait_past(act, m2_ready[1], img * SUBS)
                act.activation(wts[:, 0:WTS_A], w_raw[:, 0:WTS_A], ACT.Identity,
                               scale=rstd[:, 0:1]).then_inc(weights_ready, 1)
                act.activation(wts[:, WTS_A:WTS], w_raw[:, WTS_A:WTS], ACT.Identity,
                               scale=rstd[:, 1:2]).then_inc(weights_ready, 1)

            def evacuate(img, s, h):
                act.wait_ge(m2_ready[h], img * SUBS + s + 1)
                if s == 0 and h == 0:
                    act.wait_ge(bias_ready, img + 1)
                if s % 2 == 0 and h == 0:
                    act.wait_ge(q_ready, img * SUBS + s + 2)
                dst = rows(img, s, h * TILE_ROWS, TILE_ROWS)[:, 2, :, :].rearrange("p r c -> p (r c)")
                act.activation(dst, m2[:, h, :], ACT.Identity, bias=bias[:, 1:2]).then_inc(m2_evacuated[h], 1)

            plan = {(0, 0): (0, 0), (0, 1): (0, 1), (2, 0): (1, 0), (2, 1): (1, 1),
                    (4, 0): (2, 0), (4, 1): (2, 1), (5, 1): (3, 0), (6, 0): (3, 1)}

            def image(img, last=False):
                for s in range(SUBS):
                    if s == SUBS - 1 and not last:
                        pads_and_std(img + 1)
                    for h in range(2):
                        evacuate(img, s, h)
                        if (s, h) in plan and not last:
                            k, kind = plan[(s, h)]
                            statistics(img + 1, k, (kind,))
                if not last:
                    scale_weights(img + 1)

            act.wait_ge(zeros_ready, 1)
            act.wait_ge(consts_loaded, 64)
            for k in range(STEPS):
                statistics(0, k, (0, 1))
            pads_and_std(0)
            scale_weights(0)
            image(0)
            with act.Fori(1, B - 1) as img:
                image(img)
            image(B - 1, last=True)

        @block.vector
        def _(dve):
            def sum_partials(img):
                dve.wait_ge(partial_ready, (img + 1) * STATS)
                dve.tensor_reduce(sums[:, :, 0], partials[:, :, 0:2, :].rearrange("p s t k -> p s (t k)"),
                                  AX.X, ALU.add)
                dve.tensor_reduce(sums[:, :, 1], partials[:, :, 2, :], AX.X, ALU.add).then_inc(sums_ready, 1)

            def mean_and_variance(img):
                dve.wait_ge(group_stats_ready, img + 1)
                dve.tensor_copy(mean[:, 0:2], group_stats[:, 0, 0:1].broadcast_to([P, 2]))
                dve.tensor_copy(mean[:, 2:3], group_stats[:, 1, 0:1]).then_inc(mean_ready, 1)
                dve.wait_ge(mean_ready, img + 1)
                dve.tensor_tensor(square_mean[:, :], mean[:, 1:3], mean[:, 1:3], ALU.mult).then_inc(prep_step, 1)
                dve.wait_ge(prep_step, img * PREP + 1)
                dve.tensor_tensor(var[:, :], group_stats[:, :, 1], square_mean[:, :],
                                  ALU.subtract).then_inc(prep_step, 1)
                dve.wait_ge(prep_step, img * PREP + 2)
                dve.tensor_scalar(var_eps[:, :], var[:, :], 0.0, GN_EPS, ALU.max, ALU.add).then_inc(var_ready, 1)

            def reciprocal_std(img):
                dve.wait_ge(std_ready, img + 1)
                dve.reciprocal(rstd0[:, :], std[:, :]).then_inc(prep_step, 1)

            def newton_square(img):
                dve.wait_ge(prep_step, img * PREP + 3)
                dve.tensor_tensor(rstd_sq[:, :], rstd0[:, :], rstd0[:, :], ALU.mult).then_inc(prep_step, 1)

            def newton_product(img):
                dve.wait_ge(prep_step, img * PREP + 4)
                dve.scalar_tensor_tensor(out=newton[:, :], in0=rstd_sq[:, :], scalar=-0.5, in1=var_eps[:, :],
                                         op0=ALU.mult, op1=ALU.mult).then_inc(prep_step, 1)

            def newton_result(img):
                dve.wait_ge(prep_step, img * PREP + 5)
                dve.scalar_tensor_tensor(out=rstd[:, :], in0=newton[:, :], scalar=1.5, in1=rstd0[:, :],
                                         op0=ALU.add, op1=ALU.mult).then_inc(rstd_ready, 1)

            def total_bias(img):
                dve.wait_ge(bias_sums_ready, img + 1)
                wait_past(dve, m2_evacuated[1], img * SUBS)
                wait_past(dve, m1_evacuated[1], img * SUBS)
                dve.tensor_tensor(bias[:, :], bias_raw[:, :], bias_sums, ALU.subtract).then_inc(bias_ready, 1)

            def neighbours(img, s):
                g = img * SUBS + s
                if s % 2 == 0:
                    k = s // 2
                    dve.wait_ge(loaded[k], load_count(k) * (img + 1))
                if s == 0:
                    dve.wait_ge(top_pads_ready, img + 1)
                if s == SUBS - 1:
                    dve.wait_ge(bottom_pads_ready, img + 1)
                wait_past(dve, s_ready, g)
                x9 = rows(img, s, -1, SUB_ROWS + 2)
                up, here = x9[:, :, 0:SUB_ROWS + 1, :], x9[:, :, 1:SUB_ROWS + 2, :]
                m = mean[:, :].unsqueeze(2).broadcast_to([P, STREAMS, SUB_ROWS + 1])
                dve.tensor_tensor(q[:, :, :, 0], up[:, :, :, 0], m, ALU.add)
                dve.tensor_tensor(q[:, :, :, W], here[:, :, :, W - 1], m, ALU.add)
                dve.tensor_tensor(q[:, :, :, 1:W], up[:, :, :, 1:W], here[:, :, :, 0:W - 1],
                                  ALU.add).then_inc(q_ready, 1)

            def neighbour_sum(img, s):
                g = img * SUBS + s
                dve.wait_ge(q_ready, g + 1)
                if s > 0:
                    wait_past(dve, m2_ready[1], g - 1)
                zs = z[:, s % 2, :, :].rearrange("p t (r c) -> p t r c", c=W)
                dve.tensor_tensor(zs, q[:, :, 0:SUB_ROWS, 0:W], q[:, :, 1:SUB_ROWS + 1, 1:QW],
                                  ALU.add).then_inc(s_ready, 1)

            def stencil(img, s):
                dve.wait_ge(s_ready, img * SUBS + s + 1)
                here = rows(img, s, 0, SUB_ROWS).rearrange("p t r c -> p t (r c)")
                dve.scalar_tensor_tensor(out=z[:, s % 2, :, :], in0=here, scalar=5.0, in1=z[:, s % 2, :, :],
                                         op0=ALU.mult, op1=ALU.subtract).then_inc(z_ready, 1)

            def evacuate(img, s, h):
                dve.wait_ge(m1_ready[h], img * SUBS + s + 1)
                if s == 0 and h == 0:
                    dve.wait_ge(bias_ready, img + 1)
                if s % 2 == 0:
                    dve.wait_ge(q_ready, img * SUBS + s + 2)
                dst = rows(img, s, h * TILE_ROWS, TILE_ROWS)[:, 0:2, :, :].rearrange("p t r c -> p t (r c)")
                dve.scalar_tensor_tensor(out=dst, in0=m1[:, h, :, :], scalar=bias[:, 0:1], in1=dst,
                                         op0=ALU.add, op1=ALU.add).then_inc(m1_evacuated[h], 1)

            def image(img, last=False):
                for s in range(SUBS):
                    if s == 0:
                        neighbours(img, 1)
                        total_bias(img)
                        evacuate(img, 0, 0)
                        neighbour_sum(img, 1)
                        evacuate(img, 0, 1)
                        stencil(img, 1)
                    elif s < SUBS - 1:
                        neighbours(img, s + 1)
                        evacuate(img, s, 0)
                        neighbour_sum(img, s + 1)
                        evacuate(img, s, 1)
                        stencil(img, s + 1)
                    elif last:
                        evacuate(img, s, 0)
                        evacuate(img, s, 1)
                    else:
                        sum_partials(img + 1)
                        mean_and_variance(img + 1)
                        evacuate(img, s, 0)
                        reciprocal_std(img + 1)
                        neighbours(img + 1, 0)
                        newton_square(img + 1)
                        evacuate(img, s, 1)
                        newton_product(img + 1)
                        neighbour_sum(img + 1, 0)
                        newton_result(img + 1)
                        stencil(img + 1, 0)

            sum_partials(0)
            mean_and_variance(0)
            reciprocal_std(0)
            neighbours(0, 0)
            newton_square(0)
            newton_product(0)
            neighbour_sum(0, 0)
            newton_result(0)
            stencil(0, 0)
            dve.wait_ge(consts_loaded, 64)
            image(0)
            with dve.Fori(1, B - 1) as img:
                image(img)
            image(B - 1, last=True)

        @block.tensor
        def _(pe):
            w_aa, w_ab = wts[:, 0:CA], wts[:, CA:C]
            w_ba = wts[:, WTS_A:WTS_A + WTS_BA]
            w_bb = wts[:, WTS_A + WTS_BA:WTS]

            def group_averages(img):
                pe.wait_ge(sums_ready, img + 1)
                wait_past(pe, bias_ready, img)
                for g in range(2):
                    pe.matmul(group_stats[:, g, :], gavg[:, 2 * g, :], sums[:, :, 0], start=True, stop=False)
                    mm = pe.matmul(group_stats[:, g, :], gavg[:, 2 * g + 1, :], sums[:, :, 1],
                                   start=False, stop=True)
                mm.then_inc(group_stats_ready, 1)

            def mean_through_weights(img):
                pe.matmul(bias_sums[:, 0:1], w_aa, mean[:, 0:1], start=True, stop=False)
                pe.matmul(bias_sums[:, 0:1], w_ba[0:CB, :], mean[0:CB, 2:3], start=False, stop=True)
                pe.matmul(bias_sums[:, 1:2], w_bb, mean[:, 2:3], start=True, stop=False)
                pe.matmul(bias_sums[0:CB, 1:2], w_ab, mean[:, 0:1], start=False, stop=True)
                pe.matmul(bias_sums[CB:P, 1:2], w_ab, mean[:, 0:1], start=False,
                          stop=True).then_inc(bias_sums_ready, 1)

            def mix_to_a(img, s, h):
                zt = z[:, s % 2, :, h * TILE:(h + 1) * TILE]
                wait_past(pe, m1_evacuated[h], img * SUBS + s)
                if s == 0 and h == 0:
                    pe.wait_ge(weights_ready, 2 * img + 1)
                pe.matmul(m1[:, h, 0, :], w_aa, zt[:, 0, :], start=True, stop=False)
                pe.matmul(m1[:, h, 1, :], w_aa, zt[:, 1, :], start=True, stop=False)
                if s == 0 and h == 0:
                    pe.wait_ge(weights_ready, 2 * img + 2)
                pe.matmul(m1[:, h, 0, :], w_ba[0:CB, :], zt[0:CB, 2, :], start=False, stop=True)
                pe.matmul(m1[:, h, 1, :], w_ba[CB:P, :], zt[CB:P, 2, :], start=False,
                          stop=True).then_inc(m1_ready[h], 1)

            def mix_to_b(img, s, h):
                zt = z[:, s % 2, :, h * TILE:(h + 1) * TILE]
                xt = rows(img, s, h * TILE_ROWS, TILE_ROWS)[:, 2, :, :].rearrange("p r c -> p (r c)")
                wait_past(pe, m2_evacuated[h], img * SUBS + s)
                pe.matmul(m2[:, h, :], w_bb, zt[:, 2, :], start=True, stop=False)
                pe.matmul(m2[:, h, :], ident[:, :], xt, start=False, stop=False)
                pe.matmul(m2[0:CB, h, :], w_ab, zt[:, 0, :], start=False, stop=True)
                pe.matmul(m2[CB:P, h, :], w_ab, zt[:, 1, :], start=False, stop=True).then_inc(m2_ready[h], 1)

            def image(img, last=False):
                for s in range(SUBS):
                    if s == SUBS - 1 and not last:
                        group_averages(img + 1)
                    pe.wait_ge(z_ready, img * SUBS + s + 1)
                    mix_to_a(img, s, 0)
                    if s == 0:
                        mean_through_weights(img)
                    mix_to_a(img, s, 1)
                    mix_to_b(img, s, 0)
                    mix_to_b(img, s, 1)

            pe.wait_ge(consts_loaded, 64)
            group_averages(0)
            image(0)
            with pe.Fori(1, B - 1) as img:
                image(img)
            image(B - 1, last=True)


def group_average_matrices():
    a = np.arange(CA)
    b = CA + np.arange(P) % CB
    share = np.float32(1.0 / (GROUP_CHANNELS * H * W))
    same = [(k[:, None] // GROUP_CHANNELS == m[None, :] // GROUP_CHANNELS)
            for k, m in ((a, a), (b, a), (a, b), (b, b))]
    return np.where(np.stack(same, axis=1), share, np.float32(0.0))


def kernel(x, L0_conv_merge_w, L0_conv_merge_b):
    import concourse.bacc as bacc
    from concourse.bass_utils import run_bass_kernel_spmd

    x = np.ascontiguousarray(x)
    w = np.asarray(L0_conv_merge_w).reshape(C, C).T
    b = np.asarray(L0_conv_merge_b)
    w_lhst = np.zeros((P, WTS), w.dtype)
    w_lhst[:, 0:C] = w[0:CA, :]
    for half in range(2):
        part = slice(half * CB, (half + 1) * CB)
        w_lhst[part, WTS_A:WTS_A + WTS_BA] = w[CA:C, 0:CA]
        w_lhst[part, WTS_A + WTS_BA + half * CB:WTS_A + WTS_BA + (half + 1) * CB] = w[CA:C, CA:C]
    bias_cols = np.stack([b[0:CA], np.concatenate([b[CA:C], b[CA:C]])], axis=1)

    nc = bacc.Bacc("TRN2", target_bir_lowering=False, num_devices=1)
    arrays = {
        "x_dram": x,
        "w_lhst_dram": w_lhst,
        "bias_cols_dram": np.ascontiguousarray(bias_cols),
        "group_avg_dram": np.ascontiguousarray(group_average_matrices()),
        "identity_dram": np.eye(P, dtype=np.float32),
    }
    args = [nc.dram_tensor(n, a.shape, mybir.dt.from_np(a.dtype), kind="ExternalInput").ap()
            for n, a in arrays.items()]
    args.append(nc.dram_tensor("out_dram", (B, C, H, W), F32, kind="ExternalOutput").ap())
    conv_preact_kernel(nc, *args)
    r = run_bass_kernel_spmd(nc, [arrays], core_ids=[0])
    return r.results[0]["out_dram"]
```

```python
from contextlib import ExitStack

import numpy as np

import concourse.bass as bass
from concourse import mybir
from concourse.alu_op_type import AluOpType as ALU

F32 = mybir.dt.float32
U8 = mybir.dt.uint8
ACT = mybir.ActivationFunctionType
AX = mybir.AxisListType

B, C, H, W = 16, 192, 128, 128
GROUPS = 32
GROUP_CHANNELS = C // GROUPS
GN_EPS = 1e-5

P = 128
CA = 128
CB = C - CA
HALF = H // 2
STREAMS = 3
SLOT_ROWS = 16
ROWS = SLOT_ROWS + 2
STEPS = HALF // SLOT_ROWS
STREAM = ROWS * W
SLOT = STREAMS * STREAM
RING = 6
SUB_ROWS = 8
SUBS = HALF // SUB_ROWS
SUB = SUB_ROWS * W
TILE_ROWS = SUB_ROWS // 2
TILE = TILE_ROWS * W
QW = W + 1
WTS_A, WTS_BA, WTS_BB = C, CA, P
WTS = WTS_A + WTS_BA + WTS_BB
PREP = 5


def conv_preact_kernel(nc: bass.Bass, x, w_lhst, bias_cols, group_avg, identity, out):
    x_flat = x.rearrange("b c h w -> b c (h w)")
    out_flat = out.rearrange("b c h w -> b c (h w)")
    x_half = x.rearrange("b c (u h) w -> b c u (h w)", u=2)
    out_half = out.rearrange("b c (u h) w -> b c u (h w)", u=2)

    with ExitStack() as ctx:
        def sb(name, shape, dt=F32):
            return ctx.enter_context(nc.sbuf_tensor(name, shape, dt))

        def pb(name, shape):
            return ctx.enter_context(nc.psum_tensor(name, shape, F32))

        def sem(name):
            return ctx.enter_context(nc.semaphore(name))

        ring = sb("ring", [P, RING * SLOT])
        q = sb("q", [P, STREAMS, SUB_ROWS + 1, QW])
        z = sb("z", [P, 2, STREAMS, SUB])
        unused = sb("unused", [P, SUB], U8)
        w_raw = sb("w_raw", [P, WTS])
        wts = sb("wts", [P, WTS])
        gavg = sb("gavg", [P, 4, P])
        ident = sb("ident", [P, P])
        zeros = sb("zeros", [P, W])
        bias_raw = sb("bias_raw", [P, 2])
        bias = sb("bias", [P, 2])
        partials = sb("partials", [P, 2, STREAMS, SUBS])
        sums = sb("sums", [P, 2, 2])
        mean = sb("mean", [P, STREAMS])
        square_mean = sb("square_mean", [P, 2])
        var = sb("var", [P, 2])
        var_eps = sb("var_eps", [P, 2])
        std = sb("std", [P, 2])
        rstd0 = sb("rstd0", [P, 2])
        rstd_sq = sb("rstd_sq", [P, 2])
        newton = sb("newton", [P, 2])
        rstd = sb("rstd", [P, 2])
        mean_rstd = sb("mean_rstd", [P, 2])

        m1 = pb("m1", [P, 2, 2, TILE])
        m2 = pb("m2", [P, 2, TILE])
        small = pb("small", [P, 512])
        group_stats = small[:, 0:4].rearrange("p (g s) -> p g s", g=2)
        bias_sums = small[:, 4:6]

        consts_loaded = sem("consts_loaded")
        zeros_ready = sem("zeros_ready")
        loaded = [sem(f"loaded{k}") for k in range(STEPS)]
        stored = sem("stored")
        partial_ready = sem("partial_ready")
        sums_ready = sem("sums_ready")
        group_stats_ready = sem("group_stats_ready")
        mean_ready = sem("mean_ready")
        prep_step = sem("prep_step")
        var_ready = sem("var_ready")
        std_ready = sem("std_ready")
        rstd_ready = sem("rstd_ready")
        mean_rstd_ready = sem("mean_rstd_ready")
        first_sums_ready = sem("first_sums_ready")
        q_inside_ready = sem("q_inside_ready")
        q_carried = sem("q_carried")
        top_pads_ready = sem("top_pads_ready")
        bottom_pads_ready = sem("bottom_pads_ready")
        weights_ready = sem("weights_ready")
        bias_sums_ready = sem("bias_sums_ready")
        bias_ready = sem("bias_ready")
        q_ready = sem("q_ready")
        s_ready = sem("s_ready")
        z_ready = sem("z_ready")
        m1_ready = sem("m1_ready")
        m2_ready = [sem(f"m2_ready{h}") for h in range(2)]
        m1_evacuated = sem("m1_evacuated")
        m2_evacuated = [sem(f"m2_evacuated{h}") for h in range(2)]

        def load_count(k):
            return 16 * (4 if k in (0, STEPS - 1) else 3)

        STATS = 2 * STREAMS * SUBS
        CARRIES = SUBS - 1

        def slot(img, k, turn=0):
            base = ((img * STEPS + (k + turn)) % RING) * SLOT
            return ring[:, bass.ds(base, SLOT)].rearrange("p (t r c) -> p t r c", t=STREAMS, r=ROWS)

        def rows(img, s, first, count):
            r = 1 + (s * SUB_ROWS) % SLOT_ROWS + first
            return slot(img, s * SUB_ROWS // SLOT_ROWS)[:, :, r:r + count, :]

        def wait_past(engine, semaphore, count):
            if not isinstance(count, int) or count > 0:
                engine.wait_ge(semaphore, count)

        block = ctx.enter_context(nc.Block())

        @block.sync
        def _(sp):
            def load(img, k):
                dst = slot(img, k)
                r0 = k * SLOT_ROWS - 1
                bot0 = 0 if k == 0 else 1
                bot1 = ROWS - 1 if k == STEPS - 1 else ROWS
                if 0 < k < STEPS - 1:
                    sp.dma_start(dst[:, 0:2, 1:ROWS, :].rearrange("p t r c -> p t (r c)"),
                                 x_half[img, 0:CA, :, (r0 + 1) * W:(r0 + ROWS) * W]).then_inc(loaded[k], 16)
                else:
                    sp.dma_start(dst[:, 0, 1:ROWS, :].rearrange("p r c -> p (r c)"),
                                 x_flat[img, 0:CA, (r0 + 1) * W:(r0 + ROWS) * W]).then_inc(loaded[k], 16)
                    sp.dma_start(dst[:, 1, bot0:bot1, :].rearrange("p r c -> p (r c)"),
                                 x_flat[img, 0:CA, (HALF + r0 + bot0) * W:(HALF + r0 + bot1) * W]
                                 ).then_inc(loaded[k], 16)
                sp.dma_start(dst[0:CB, 2, 1:ROWS, :].rearrange("p r c -> p (r c)"),
                             x_flat[img, CA:C, (r0 + 1) * W:(r0 + ROWS) * W]).then_inc(loaded[k], 16)
                sp.dma_start(dst[CB:P, 2, bot0:bot1, :].rearrange("p r c -> p (r c)"),
                             x_flat[img, CA:C, (HALF + r0 + bot0) * W:(HALF + r0 + bot1) * W]
                             ).then_inc(loaded[k], 16)

            def store(img, s, k=None):
                sp.wait_ge(m1_evacuated, img * SUBS + s + 1)
                sp.wait_ge(m2_evacuated[1], img * SUBS + s + 1)
                src = rows(img, s, 0, SUB_ROWS)
                a, b = s * SUB, (s + 1) * SUB
                sp.dma_start(out_half[img, 0:CA, :, a:b],
                             src[:, 0:2, :, :].rearrange("p t r c -> p t (r c)")).then_inc(stored, 16)
                if k is not None:
                    before = k + RING - STEPS
                    sp.wait_ge(loaded[before % STEPS], load_count(before % STEPS) * (img + before // STEPS + 1))
                sp.dma_start(out_half[img, CA:C, 0, a:b],
                             src[0:CB, 2, :, :].rearrange("p r c -> p (r c)")).then_inc(stored, 16)
                sp.dma_start(out_half[img, CA:C, 1, a:b],
                             src[CB:P, 2, :, :].rearrange("p r c -> p (r c)")).then_inc(stored, 16)

            def image(img, loads):
                for k in range(STEPS):
                    subs = SUBS // STEPS
                    for s in range(k * subs, (k + 1) * subs):
                        store(img, s, k if k in loads and s % subs == 0 else None)
                    if k in loads:
                        sp.wait_ge(stored, 48 * (img * SUBS + (k + 1) * subs))
                        ahead = k + RING
                        load(img + ahead // STEPS, ahead % STEPS)

            sp.dma_start(w_raw[:, :], w_lhst).then_inc(consts_loaded, 16)
            sp.dma_start(gavg[:, :, :], group_avg).then_inc(consts_loaded, 16)
            sp.dma_start(ident[:, :], identity).then_inc(consts_loaded, 16)
            sp.dma_start(bias_raw[:, :], bias_cols).then_inc(consts_loaded, 16)
            for t in range(RING):
                if t >= STEPS:
                    sp.wait_ge(loaded[t % STEPS], load_count(t % STEPS))
                load(t // STEPS, t % STEPS)
            image(0, range(STEPS))
            with sp.Fori(1, B - 2) as img:
                image(img, range(STEPS))
            image(B - 2, range(RING - STEPS))
            image(B - 1, ())
            sp.wait_ge(stored, 48 * B * SUBS)

        @block.gpsimd
        def _(pool):
            pool.memset(zeros[:, :], 0.0).then_inc(zeros_ready, 1)

        @block.scalar
        def _(act):
            def statistics(img, first, count, kinds=(0, 1)):
                ops = [(k, kind, t, half) for k in range(STEPS) for kind in kinds
                       for t in range(STREAMS) for half in range(2)]
                done = 0 if len(kinds) == 1 else img * STATS - STATS // 2
                for n, (k, kind, t, half) in list(enumerate(ops))[first:first + count]:
                    if n % (len(ops) // STEPS) == 0:
                        act.wait_ge(loaded[k], load_count(k) * (img + 1))
                    if n == 0:
                        wait_past(act, sums_ready, img)
                    wait_past(act, partial_ready, done + n)
                    r0 = 1 + half * SUB_ROWS
                    act.activation(unused[:, :],
                                   slot(img, k, RING * kind)[:, t, r0:r0 + SUB_ROWS, :].rearrange("p r c -> p (r c)"),
                                   ACT.Square if kind else ACT.Identity,
                                   accum_out=partials[:, kind, t, 2 * k + half:2 * k + half + 1]
                                   ).then_inc(partial_ready, 1)

            def pads_and_std(img):
                act.wait_ge(mean_ready, img + 1)
                top, bottom = slot(img, 0), slot(img, STEPS - 1)
                act.activation(top[:, 0, 0, :], zeros[:, :], ACT.Identity, bias=mean[:, 0:1])
                act.activation(top[0:CB, 2, 0, :], zeros[0:CB, :], ACT.Identity,
                               bias=mean[0:CB, 2:3]).then_inc(top_pads_ready, 1)
                act.wait_ge(var_ready, img + 1)
                act.activation(std[:, :], var_eps[:, :], ACT.Sqrt).then_inc(std_ready, 1)
                act.activation(bottom[:, 1, ROWS - 1, :], zeros[:, :], ACT.Identity, bias=mean[:, 1:2])
                act.activation(bottom[CB:P, 2, ROWS - 1, :], zeros[CB:P, :], ACT.Identity,
                               bias=mean[CB:P, 2:3]).then_inc(bottom_pads_ready, 1)

            def scale_weights(img):
                act.wait_ge(rstd_ready, img + 1)
                wait_past(act, m2_ready[1], img * SUBS)
                act.activation(wts[:, 0:WTS_A], w_raw[:, 0:WTS_A], ACT.Identity,
                               scale=rstd[:, 0:1]).then_inc(weights_ready, 1)
                act.activation(wts[:, WTS_A:WTS], w_raw[:, WTS_A:WTS], ACT.Identity,
                               scale=rstd[:, 1:2]).then_inc(weights_ready, 1)

            def carry(img, s):
                act.wait_ge(s_ready, img * SUBS + s + 1)
                act.activation(q[:, :, 0, :], q[:, :, SUB_ROWS, :], ACT.Identity).then_inc(q_carried, 1)

            def evacuate(img, s, h):
                act.wait_ge(m2_ready[h], img * SUBS + s + 1)
                if s == 0 and h == 0:
                    act.wait_ge(bias_ready, img + 1)
                dst = rows(img, s, h * TILE_ROWS, TILE_ROWS)[:, 2, :, :].rearrange("p r c -> p (r c)")
                act.activation(dst, m2[:, h, :], ACT.Identity, bias=bias[:, 1:2]).then_inc(m2_evacuated[h], 1)

            per_tile = (2, 6)
            assert STATS % sum(per_tile) == 0 and STATS // sum(per_tile) < SUBS - 1

            def image(img, last=False):
                for s in range(SUBS):
                    if s < CARRIES - 1:
                        carry(img, s + 1)
                    elif s == SUBS - 1 and not last:
                        pads_and_std(img + 1)
                        carry(img + 1, 0)
                    for h in range(2):
                        evacuate(img, s, h)
                        first = sum(per_tile) * s + sum(per_tile[:h])
                        if first < STATS and not last:
                            statistics(img + 1, first, per_tile[h])
                if not last:
                    scale_weights(img + 1)

            act.wait_ge(zeros_ready, 1)
            act.wait_ge(consts_loaded, 64)
            statistics(0, 0, STATS // 2, kinds=(1,))
            pads_and_std(0)
            carry(0, 0)
            scale_weights(0)
            image(0)
            with act.Fori(1, B - 1) as img:
                image(img)
            image(B - 1, last=True)

        @block.vector
        def _(dve):
            def sum_partials(img):
                dve.wait_ge(partial_ready, img * STATS + STATS // 2)
                dve.tensor_reduce(sums[:, :, 0], partials[:, :, 0:2, :].rearrange("p s t k -> p s (t k)"),
                                  AX.X, ALU.add)
                dve.tensor_reduce(sums[:, :, 1], partials[:, :, 2, :], AX.X, ALU.add).then_inc(sums_ready, 1)

            def mean_and_variance(img):
                dve.wait_ge(group_stats_ready, img + 1)
                dve.tensor_copy(mean[:, 0:2], group_stats[:, 0, 0:1].broadcast_to([P, 2]))
                dve.tensor_copy(mean[:, 2:3], group_stats[:, 1, 0:1]).then_inc(mean_ready, 1)
                dve.wait_ge(mean_ready, img + 1)
                dve.tensor_tensor(square_mean[:, :], mean[:, 1:3], mean[:, 1:3], ALU.mult).then_inc(prep_step, 1)
                dve.wait_ge(prep_step, img * PREP + 1)
                dve.tensor_tensor(var[:, :], group_stats[:, :, 1], square_mean[:, :],
                                  ALU.subtract).then_inc(prep_step, 1)
                dve.wait_ge(prep_step, img * PREP + 2)
                dve.tensor_scalar(var_eps[:, :], var[:, :], 0.0, GN_EPS, ALU.max, ALU.add).then_inc(var_ready, 1)

            def reciprocal_std(img):
                dve.wait_ge(std_ready, img + 1)
                dve.reciprocal(rstd0[:, :], std[:, :]).then_inc(prep_step, 1)

            def newton_square(img):
                dve.wait_ge(prep_step, img * PREP + 3)
                dve.tensor_tensor(rstd_sq[:, :], rstd0[:, :], rstd0[:, :], ALU.mult).then_inc(prep_step, 1)

            def newton_product(img):
                dve.wait_ge(prep_step, img * PREP + 4)
                dve.scalar_tensor_tensor(out=newton[:, :], in0=rstd_sq[:, :], scalar=-0.5, in1=var_eps[:, :],
                                         op0=ALU.mult, op1=ALU.mult).then_inc(prep_step, 1)

            def newton_result(img):
                dve.wait_ge(prep_step, img * PREP + 5)
                dve.scalar_tensor_tensor(out=rstd[:, :], in0=newton[:, :], scalar=1.5, in1=rstd0[:, :],
                                         op0=ALU.add, op1=ALU.mult).then_inc(rstd_ready, 1)

            def scaled_mean(img):
                dve.wait_ge(rstd_ready, img + 1)
                dve.tensor_tensor(mean_rstd[:, :], mean[:, 1:3], rstd[:, :], ALU.mult).then_inc(mean_rstd_ready, 1)

            def total_bias(img):
                dve.wait_ge(bias_sums_ready, img + 1)
                wait_past(dve, m2_evacuated[1], img * SUBS)
                wait_past(dve, m1_evacuated, img * SUBS)
                dve.tensor_tensor(bias[:, :], bias_raw[:, :], bias_sums, ALU.subtract).then_inc(bias_ready, 1)

            def neighbours_inside(img, s):
                if s % 2 == 0:
                    k = s // 2
                    dve.wait_ge(loaded[k], load_count(k) * (img + 1))
                if s == SUBS - 1:
                    dve.wait_ge(bottom_pads_ready, img + 1)
                if s > 0:
                    dve.wait_ge(q_carried, CARRIES * img + s)
                else:
                    wait_past(dve, s_ready, img * SUBS)
                x9 = rows(img, s, 0, SUB_ROWS + 1)
                dve.tensor_tensor(q[:, :, 1:SUB_ROWS + 1, 1:W], x9[:, :, 0:SUB_ROWS, 1:W],
                                  x9[:, :, 1:SUB_ROWS + 1, 0:W - 1], ALU.add).then_inc(q_inside_ready, 1)

            def neighbours_edges(img, s):
                first = 0 if s == 0 else 1
                count = SUB_ROWS + 1 - first
                up = rows(img, s, first - 1, count)
                here = rows(img, s, first, count)
                m = mean[:, :].unsqueeze(2).broadcast_to([P, STREAMS, count])
                if s == 0:
                    dve.wait_ge(top_pads_ready, img + 1)
                    dve.tensor_tensor(q[:, :, 0, 1:W], up[:, :, 0, 1:W], here[:, :, 0, 0:W - 1], ALU.add)
                dve.tensor_tensor(q[:, :, first:SUB_ROWS + 1, 0], up[:, :, :, 0], m, ALU.add)
                dve.tensor_tensor(q[:, :, first:SUB_ROWS + 1, W], here[:, :, :, W - 1], m,
                                  ALU.add).then_inc(q_ready, 1)

            def neighbours(img, s):
                neighbours_inside(img, s)
                neighbours_edges(img, s)

            def neighbour_sum(img, s):
                g = img * SUBS + s
                dve.wait_ge(q_ready, g + 1)
                wait_past(dve, m2_ready[1], g - 1)
                zs = z[:, s % 2, :, :].rearrange("p t (r c) -> p t r c", c=W)
                dve.tensor_tensor(zs, q[:, :, 0:SUB_ROWS, 0:W], q[:, :, 1:SUB_ROWS + 1, 1:QW],
                                  ALU.add).then_inc(s_ready, 1)

            def stencil(img, s):
                dve.wait_ge(s_ready, img * SUBS + s + 1)
                here = rows(img, s, 0, SUB_ROWS).rearrange("p t r c -> p t (r c)")
                dve.scalar_tensor_tensor(out=z[:, s % 2, :, :], in0=here, scalar=5.0, in1=z[:, s % 2, :, :],
                                         op0=ALU.mult, op1=ALU.subtract).then_inc(z_ready, 1)

            def evacuate(img, s):
                dve.wait_ge(m1_ready, img * SUBS + s + 1)
                if s == 0:
                    dve.wait_ge(bias_ready, img + 1)
                dst = rows(img, s, 0, SUB_ROWS)[:, 0:2, :, :].rearrange("p t r c -> p t (r c)")
                dve.scalar_tensor_tensor(out=dst, in0=m1[:, :, :, :].rearrange("p t h c -> p t (h c)"),
                                         scalar=bias[:, 0:1], in1=dst,
                                         op0=ALU.add, op1=ALU.add).then_inc(m1_evacuated, 1)

            def image(img, last=False):
                for s in range(SUBS):
                    if s < SUBS - 1:
                        neighbours(img, s + 1)
                        neighbour_sum(img, s + 1)
                        stencil(img, s + 1)
                        if s == 0:
                            total_bias(img)
                        evacuate(img, s)
                    elif last:
                        evacuate(img, s)
                    else:
                        sum_partials(img + 1)
                        neighbours_inside(img + 1, 0)
                        mean_and_variance(img + 1)
                        neighbours_edges(img + 1, 0)
                        reciprocal_std(img + 1)
                        neighbour_sum(img + 1, 0)
                        newton_square(img + 1)
                        newton_product(img + 1)
                        newton_result(img + 1)
                        scaled_mean(img + 1)
                        evacuate(img, s)
                        stencil(img + 1, 0)

            def first_sums(k):
                dve.wait_ge(loaded[k], load_count(k))
                for t in range(STREAMS):
                    whole = slot(0, k)[:, t, 1:1 + SLOT_ROWS, :].rearrange("p (u r) c -> p u (r c)", u=2)
                    dve.tensor_reduce(partials[:, 0, t, 2 * k:2 * k + 2], whole, AX.X,
                                      ALU.add).then_inc(first_sums_ready, 1)

            for k in range(STEPS):
                first_sums(k)
            dve.wait_ge(first_sums_ready, STREAMS * STEPS)
            sum_partials(0)
            neighbours_inside(0, 0)
            mean_and_variance(0)
            neighbours_edges(0, 0)
            reciprocal_std(0)
            newton_square(0)
            neighbour_sum(0, 0)
            newton_product(0)
            newton_result(0)
            scaled_mean(0)
            stencil(0, 0)
            dve.wait_ge(consts_loaded, 64)
            image(0)
            with dve.Fori(1, B - 1) as img:
                image(img)
            image(B - 1, last=True)

        @block.tensor
        def _(pe):
            w_aa, w_ab = wts[:, 0:CA], wts[:, CA:C]
            w_ba = wts[:, WTS_A:WTS_A + WTS_BA]
            w_bb = wts[:, WTS_A + WTS_BA:WTS]

            def group_averages(img):
                pe.wait_ge(sums_ready, img + 1)
                wait_past(pe, bias_ready, img)
                for g in range(2):
                    pe.matmul(group_stats[:, g, :], gavg[:, 2 * g, :], sums[:, :, 0], start=True, stop=False)
                    mm = pe.matmul(group_stats[:, g, :], gavg[:, 2 * g + 1, :], sums[:, :, 1],
                                   start=False, stop=True)
                mm.then_inc(group_stats_ready, 1)

            def mean_through_weights(img):
                pe.wait_ge(mean_rstd_ready, img + 1)
                m_a, m_b = mean_rstd[:, 0:1], mean_rstd[:, 1:2]
                pe.matmul(bias_sums[:, 0:1], w_raw[:, 0:CA], m_a, start=True, stop=False)
                pe.matmul(bias_sums[:, 0:1], w_raw[0:CB, WTS_A:WTS_A + WTS_BA], m_b[0:CB, :], start=False, stop=True)
                pe.matmul(bias_sums[:, 1:2], w_raw[:, WTS_A + WTS_BA:WTS], m_b, start=True, stop=False)
                pe.matmul(bias_sums[0:CB, 1:2], w_raw[:, CA:C], m_a, start=False, stop=True)
                pe.matmul(bias_sums[CB:P, 1:2], w_raw[:, CA:C], m_a, start=False,
                          stop=True).then_inc(bias_sums_ready, 1)

            def mix_to_a(img, s, h):
                zt = z[:, s % 2, :, h * TILE:(h + 1) * TILE]
                if h == 0:
                    wait_past(pe, m1_evacuated, img * SUBS + s)
                if s == 0 and h == 0:
                    pe.wait_ge(weights_ready, 2 * img + 1)
                pe.matmul(m1[:, 0, h, :], w_aa, zt[:, 0, :], start=True, stop=False)
                pe.matmul(m1[:, 1, h, :], w_aa, zt[:, 1, :], start=True, stop=False)
                if s == 0 and h == 0:
                    pe.wait_ge(weights_ready, 2 * img + 2)
                pe.matmul(m1[:, 0, h, :], w_ba[0:CB, :], zt[0:CB, 2, :], start=False, stop=True)
                mm = pe.matmul(m1[:, 1, h, :], w_ba[CB:P, :], zt[CB:P, 2, :], start=False, stop=True)
                if h == 1:
                    mm.then_inc(m1_ready, 1)

            def mix_to_b(img, s, h):
                zt = z[:, s % 2, :, h * TILE:(h + 1) * TILE]
                xt = rows(img, s, h * TILE_ROWS, TILE_ROWS)[:, 2, :, :].rearrange("p r c -> p (r c)")
                wait_past(pe, m2_evacuated[h], img * SUBS + s)
                pe.matmul(m2[:, h, :], w_bb, zt[:, 2, :], start=True, stop=False)
                pe.matmul(m2[:, h, :], ident[:, :], xt, start=False, stop=False)
                pe.matmul(m2[0:CB, h, :], w_ab, zt[:, 0, :], start=False, stop=True)
                pe.matmul(m2[CB:P, h, :], w_ab, zt[:, 1, :], start=False, stop=True).then_inc(m2_ready[h], 1)

            def image(img, last=False):
                for s in range(SUBS):
                    if s == SUBS - 1 and not last:
                        group_averages(img + 1)
                    if s == 0:
                        mean_through_weights(img)
                    pe.wait_ge(z_ready, img * SUBS + s + 1)
                    mix_to_a(img, s, 0)
                    mix_to_a(img, s, 1)
                    mix_to_b(img, s, 0)
                    mix_to_b(img, s, 1)

            pe.wait_ge(consts_loaded, 64)
            group_averages(0)
            image(0)
            with pe.Fori(1, B - 1) as img:
                image(img)
            image(B - 1, last=True)


def group_average_matrices():
    a = np.arange(CA)
    b = CA + np.arange(P) % CB
    share = np.float32(1.0 / (GROUP_CHANNELS * H * W))
    same = [(k[:, None] // GROUP_CHANNELS == m[None, :] // GROUP_CHANNELS)
            for k, m in ((a, a), (b, a), (a, b), (b, b))]
    return np.where(np.stack(same, axis=1), share, np.float32(0.0))


def kernel(x, L0_conv_merge_w, L0_conv_merge_b):
    import concourse.bacc as bacc
    from concourse.bass_utils import run_bass_kernel_spmd

    x = np.ascontiguousarray(x)
    w = np.asarray(L0_conv_merge_w).reshape(C, C).T
    b = np.asarray(L0_conv_merge_b)
    w_lhst = np.zeros((P, WTS), w.dtype)
    w_lhst[:, 0:C] = w[0:CA, :]
    for half in range(2):
        part = slice(half * CB, (half + 1) * CB)
        w_lhst[part, WTS_A:WTS_A + WTS_BA] = w[CA:C, 0:CA]
        w_lhst[part, WTS_A + WTS_BA + half * CB:WTS_A + WTS_BA + (half + 1) * CB] = w[CA:C, CA:C]
    bias_cols = np.stack([b[0:CA], np.concatenate([b[CA:C], b[CA:C]])], axis=1)

    nc = bacc.Bacc("TRN2", target_bir_lowering=False, num_devices=1)
    arrays = {
        "x_dram": x,
        "w_lhst_dram": w_lhst,
        "bias_cols_dram": np.ascontiguousarray(bias_cols),
        "group_avg_dram": np.ascontiguousarray(group_average_matrices()),
        "identity_dram": np.eye(P, dtype=np.float32),
    }
    args = [nc.dram_tensor(n, a.shape, mybir.dt.from_np(a.dtype), kind="ExternalInput").ap()
            for n, a in arrays.items()]
    args.append(nc.dram_tensor("out_dram", (B, C, H, W), F32, kind="ExternalOutput").ap())
    conv_preact_kernel(nc, *args)
    r = run_bass_kernel_spmd(nc, [arrays], core_ids=[0])
    return r.results[0]["out_dram"]
```

```python
from contextlib import ExitStack

import numpy as np

import concourse.bass as bass
from concourse import mybir
from concourse.alu_op_type import AluOpType as ALU

F32 = mybir.dt.float32
U8 = mybir.dt.uint8
ACT = mybir.ActivationFunctionType
AX = mybir.AxisListType

B, C, H, W = 16, 192, 128, 128
GROUPS = 32
GROUP_CHANNELS = C // GROUPS
GN_EPS = 1e-5

P = 128
CA = 128
CB = C - CA
HALF = H // 2
STREAMS = 3
SLOT_ROWS = 16
ROWS = SLOT_ROWS + 2
STEPS = HALF // SLOT_ROWS
STREAM = ROWS * W
SLOT = STREAMS * STREAM
RING = 6
SUB_ROWS = 8
SUBS = HALF // SUB_ROWS
SUB = SUB_ROWS * W
TILE_ROWS = SUB_ROWS // 2
TILE = TILE_ROWS * W
QW = W + 1
WTS_A, WTS_BA, WTS_BB = C, CA, P
WTS = WTS_A + WTS_BA + WTS_BB
GAVG_AA, GAVG_BB, GAVG_BA, GAVG_AB = P, P, P - CB, CB
GAVG = GAVG_AA + GAVG_BB + GAVG_BA + GAVG_AB
PREP = 6


def conv_preact_kernel(nc: bass.Bass, x, w_lhst, bias_cols, group_avg, identity, out):
    x_flat = x.rearrange("b c h w -> b c (h w)")
    out_flat = out.rearrange("b c h w -> b c (h w)")
    x_half = x.rearrange("b c (u h) w -> b c u (h w)", u=2)
    out_half = out.rearrange("b c (u h) w -> b c u (h w)", u=2)

    with ExitStack() as ctx:
        def sb(name, shape, dt=F32):
            return ctx.enter_context(nc.sbuf_tensor(name, shape, dt))

        def pb(name, shape):
            return ctx.enter_context(nc.psum_tensor(name, shape, F32))

        def sem(name):
            return ctx.enter_context(nc.semaphore(name))

        ring = sb("ring", [P, RING * SLOT])
        q = sb("q", [P, STREAMS, SUB_ROWS + 1, QW])
        z = sb("z", [P, 2, STREAMS, SUB])
        unused = sb("unused", [P, SLOT_ROWS * W], U8)
        w_raw = sb("w_raw", [P, WTS])
        wts = sb("wts", [P, WTS])
        gavg = sb("gavg", [P, GAVG])
        ident = sb("ident", [P, P])
        pairs = sb("pairs", [P, 13, 2])
        (mean_square, square_mean, var, var_floor, var_eps, std, rstd0, rstd_sq, newton, newton_scaled, newton_factor,
         rstd, mean_rstd) = (pairs[:, n, :] for n in range(13))
        bias_raw = sb("bias_raw", [P, 2])
        bias = sb("bias", [P, 2])
        partials = sb("partials", [P, 2, STREAMS, STEPS])
        sums = sb("sums", [P, 2, 2])
        mean = sb("mean", [P, STREAMS])
        constants = sb("constants", [P, 3, 2])
        eps, minus_half, three_halves = (constants[:, n, :] for n in range(3))

        m1 = pb("m1", [P, 2, 2, TILE])
        m2 = pb("m2", [P, 2, TILE])
        small = pb("small", [P, 512])
        group_stats = small[:, 0:4].rearrange("p (g s) -> p g s", g=2)
        bias_sums = small[:, 4:6]

        consts_loaded = sem("consts_loaded")
        constants_ready = sem("constants_ready")
        loaded = [sem(f"loaded{k}") for k in range(STEPS)]
        first_loaded = [sem(f"first_loaded{t}") for t in range(2)]
        stored = sem("stored")
        partial_ready = sem("partial_ready")
        sums_ready = sem("sums_ready")
        group_stats_ready = sem("group_stats_ready")
        mean_ready = sem("mean_ready")
        mean_square_ready = sem("mean_square_ready")
        prep_step = sem("prep_step")
        var_ready = sem("var_ready")
        var_floor_ready = sem("var_floor_ready")
        std_ready = sem("std_ready")
        rstd0_ready = sem("rstd0_ready")
        rstd_ready = sem("rstd_ready")
        mean_rstd_ready = sem("mean_rstd_ready")
        first_sums_ready = sem("first_sums_ready")
        q_inside_a_ready = sem("q_inside_a_ready")
        q_inside_b_ready = sem("q_inside_b_ready")
        q_carried = sem("q_carried")
        top_pads_ready = sem("top_pads_ready")
        bottom_pads_ready = sem("bottom_pads_ready")
        weights_to_a_ready = sem("weights_to_a_ready")
        weights_to_b_ready = sem("weights_to_b_ready")
        bias_sums_ready = sem("bias_sums_ready")
        bias_ready = sem("bias_ready")
        q_edges_ready = sem("q_edges_ready")
        s_ready = sem("s_ready")
        s_a_ready = sem("s_a_ready")
        z_ready = sem("z_ready")
        m1_ready = sem("m1_ready")
        m2_ready = [sem(f"m2_ready{h}") for h in range(2)]
        m1_evacuated = sem("m1_evacuated")
        m2_evacuated = [sem(f"m2_evacuated{h}") for h in range(2)]

        def load_count(k):
            return 16 * (4 if k in (0, STEPS - 1) else 3)

        def landed(img, k):
            return load_count(k) * (img + 1) - (32 if k == STEPS - 1 else 0)

        STATS = 2 * STREAMS * STEPS
        CARRIES = SUBS - 1

        def slot(img, k, turn=0):
            base = ((img * STEPS + (k + turn)) % RING) * SLOT
            return ring[:, bass.ds(base, SLOT)].rearrange("p (t r c) -> p t r c", t=STREAMS, r=ROWS)

        def rows(img, s, first, count):
            r = 1 + (s * SUB_ROWS) % SLOT_ROWS + first
            return slot(img, s * SUB_ROWS // SLOT_ROWS)[:, :, r:r + count, :]

        def wait_past(engine, semaphore, count):
            if not isinstance(count, int) or count > 0:
                engine.wait_ge(semaphore, count)

        block = ctx.enter_context(nc.Block())

        @block.sync
        def _(sp):
            def load(img, k):
                dst = slot(img, k)
                r0 = k * SLOT_ROWS - 1
                bot0 = 0 if k == 0 else 1
                bot1 = ROWS - 1 if k == STEPS - 1 else ROWS
                if 0 < k < STEPS - 1:
                    sp.dma_start(dst[:, 0:2, 1:ROWS, :].rearrange("p t r c -> p t (r c)"),
                                 x_half[img, 0:CA, :, (r0 + 1) * W:(r0 + ROWS) * W]).then_inc(loaded[k], 16)
                else:
                    own = isinstance(img, int) and img == 0 and k == STEPS - 1
                    top_loaded, bottom_loaded = first_loaded if own else (loaded[k], loaded[k])
                    sp.dma_start(dst[:, 0, 1:ROWS, :].rearrange("p r c -> p (r c)"),
                                 x_flat[img, 0:CA, (r0 + 1) * W:(r0 + ROWS) * W]).then_inc(top_loaded, 16)
                    sp.dma_start(dst[:, 1, bot0:bot1, :].rearrange("p r c -> p (r c)"),
                                 x_flat[img, 0:CA, (HALF + r0 + bot0) * W:(HALF + r0 + bot1) * W]
                                 ).then_inc(bottom_loaded, 16)
                sp.dma_start(dst[0:CB, 2, 1:ROWS, :].rearrange("p r c -> p (r c)"),
                             x_flat[img, CA:C, (r0 + 1) * W:(r0 + ROWS) * W]).then_inc(loaded[k], 16)
                sp.dma_start(dst[CB:P, 2, bot0:bot1, :].rearrange("p r c -> p (r c)"),
                             x_flat[img, CA:C, (HALF + r0 + bot0) * W:(HALF + r0 + bot1) * W]
                             ).then_inc(loaded[k], 16)

            def store(img, s, k=None):
                sp.wait_ge(m1_evacuated, img * SUBS + s + 1)
                src = rows(img, s, 0, SUB_ROWS)
                a, b = s * SUB, (s + 1) * SUB
                sp.dma_start(out_half[img, 0:CA, :, a:b],
                             src[:, 0:2, :, :].rearrange("p t r c -> p t (r c)")).then_inc(stored, 16)
                if k is not None:
                    before = k + RING - STEPS
                    sp.wait_ge(loaded[before % STEPS], landed(img + before // STEPS, before % STEPS))
                sp.wait_ge(m2_evacuated[1], img * SUBS + s + 1)
                sp.dma_start(out_half[img, CA:C, 0, a:b],
                             src[0:CB, 2, :, :].rearrange("p r c -> p (r c)")).then_inc(stored, 16)
                sp.dma_start(out_half[img, CA:C, 1, a:b],
                             src[CB:P, 2, :, :].rearrange("p r c -> p (r c)")).then_inc(stored, 16)

            def image(img, loads):
                for k in range(STEPS):
                    subs = SUBS // STEPS
                    for s in range(k * subs, (k + 1) * subs):
                        store(img, s, k if k in loads and s % subs == 0 else None)
                    if k in loads:
                        sp.wait_ge(stored, 48 * (img * SUBS + (k + 1) * subs))
                        ahead = k + RING
                        load(img + ahead // STEPS, ahead % STEPS)

            for t in range(RING):
                if t >= STEPS:
                    sp.wait_ge(loaded[t % STEPS], landed(0, t % STEPS))
                load(t // STEPS, t % STEPS)
                if t == 0:
                    sp.dma_start(w_raw[:, :], w_lhst).then_inc(consts_loaded, 16)
                    sp.dma_start(gavg[:, :], group_avg).then_inc(consts_loaded, 16)
                    sp.dma_start(ident[:, :], identity).then_inc(consts_loaded, 16)
                    sp.dma_start(bias_raw[:, :], bias_cols).then_inc(consts_loaded, 16)
            image(0, range(STEPS))
            with sp.Fori(1, B - 2) as img:
                image(img, range(STEPS))
            image(B - 2, range(RING - STEPS))
            image(B - 1, ())
            sp.wait_ge(stored, 48 * B * SUBS)

        @block.gpsimd
        def _(pool):
            def variance(img):
                pool.wait_ge(mean_square_ready, img + 1)
                pool.tensor_tensor(square_mean, mean[:, 1:3], mean[:, 1:3], ALU.mult).then_inc(prep_step, 1)
                pool.wait_ge(prep_step, img * PREP + 1)
                pool.tensor_tensor(var, mean_square, square_mean, ALU.subtract).then_inc(var_ready, 1)

            def reciprocal_std(img):
                pool.wait_ge(rstd0_ready, img + 1)
                pool.tensor_tensor(var_eps, var_floor, eps, ALU.add).then_inc(prep_step, 1)
                pool.tensor_tensor(rstd_sq, rstd0, rstd0, ALU.mult).then_inc(prep_step, 1)
                pool.wait_ge(prep_step, img * PREP + 3)
                pool.tensor_tensor(newton, rstd_sq, var_eps, ALU.mult).then_inc(prep_step, 1)
                pool.wait_ge(prep_step, img * PREP + 4)
                pool.tensor_tensor(newton_scaled, newton, minus_half, ALU.mult).then_inc(prep_step, 1)
                pool.wait_ge(prep_step, img * PREP + 5)
                pool.tensor_tensor(newton_factor, newton_scaled, three_halves,
                                   ALU.add).then_inc(prep_step, 1)
                pool.wait_ge(prep_step, img * PREP + 6)
                pool.tensor_tensor(rstd, newton_factor, rstd0, ALU.mult).then_inc(rstd_ready, 1)
                pool.wait_ge(rstd_ready, img + 1)
                pool.tensor_tensor(mean_rstd, mean[:, 1:3], rstd, ALU.mult).then_inc(mean_rstd_ready, 1)

            def neighbours_edges(img, s):
                if s % 2 == 0:
                    k = s // 2
                    pool.wait_ge(loaded[k], landed(img, k))
                if s == SUBS - 1:
                    pool.wait_ge(bottom_pads_ready, img + 1)
                if s > 0:
                    pool.wait_ge(q_carried, CARRIES * img + s)
                else:
                    wait_past(pool, s_ready, img * SUBS)
                    pool.wait_ge(top_pads_ready, img + 1)
                first = 0 if s == 0 else 1
                count = SUB_ROWS + 1 - first
                up = rows(img, s, first - 1, count)
                here = rows(img, s, first, count)
                m = mean[:, :].unsqueeze(2).broadcast_to([P, STREAMS, count])
                if s == 0:
                    pool.tensor_tensor(q[:, :, 0, 1:W], up[:, :, 0, 1:W], here[:, :, 0, 0:W - 1], ALU.add)
                pool.tensor_tensor(q[:, :, first:SUB_ROWS + 1, 0], up[:, :, :, 0], m, ALU.add)
                pool.tensor_tensor(q[:, :, first:SUB_ROWS + 1, W], here[:, :, :, W - 1], m,
                                   ALU.add).then_inc(q_edges_ready, 1)

            def prepare(img):
                neighbours_edges(img, 0)
                variance(img)
                reciprocal_std(img)

            def image(img, last=False):
                for s in range(1, SUBS):
                    neighbours_edges(img, s)
                if not last:
                    prepare(img + 1)

            pool.memset(eps, GN_EPS)
            pool.memset(minus_half, -0.5)
            pool.memset(three_halves, 1.5).then_inc(constants_ready, 1)
            pool.wait_ge(constants_ready, 1)
            prepare(0)
            image(0)
            with pool.Fori(1, B - 1) as img:
                image(img)
            image(B - 1, last=True)

        @block.scalar
        def _(act):
            def statistics(img, first, count, kinds=(0, 1)):
                ops = [(k, kind, t) for k in range(STEPS) for kind in kinds for t in range(STREAMS)]
                done = 0 if len(kinds) == 1 else img * STATS - STATS // 2
                for n, (k, kind, t) in list(enumerate(ops))[first:first + count]:
                    if len(kinds) == 1 and k == STEPS - 1 and t < 2:
                        act.wait_ge(first_loaded[t], 16)
                    elif n % (len(ops) // STEPS) == 0 or len(kinds) == 1:
                        act.wait_ge(loaded[k], landed(img, k))
                    if n == 0:
                        wait_past(act, sums_ready, img)
                    wait_past(act, partial_ready, done + n)
                    act.activation(unused[:, :],
                                   slot(img, k, RING * kind)[:, t, 1:1 + SLOT_ROWS, :].rearrange("p r c -> p (r c)"),
                                   ACT.Square if kind else ACT.Identity,
                                   accum_out=partials[:, kind, t, k:k + 1]).then_inc(partial_ready, 1)

            def mean_pads_and_std(img):
                act.wait_ge(group_stats_ready, img + 1)
                wait_past(act, q_edges_ready, img * SUBS)
                act.activation(mean[:, 0:1], group_stats[:, 0, 0:1], ACT.Identity)
                act.activation(mean[:, 1:3], group_stats[:, :, 0], ACT.Identity).then_inc(mean_ready, 1)
                act.wait_ge(mean_ready, img + 1)
                top, bottom = slot(img, 0), slot(img, STEPS - 1)
                act.activation(top[:, 0, 0, :], ident[:, 0:W], ACT.Identity, scale=0.0, bias=mean[:, 0:1])
                act.activation(top[0:CB, 2, 0, :], ident[0:CB, 0:W], ACT.Identity, scale=0.0,
                               bias=mean[0:CB, 2:3]).then_inc(top_pads_ready, 1)
                act.activation(mean_square, group_stats[:, :, 1], ACT.Identity).then_inc(mean_square_ready, 1)
                act.wait_ge(var_ready, img + 1)
                act.activation(var_floor, var, ACT.Relu).then_inc(var_floor_ready, 1)
                act.wait_ge(var_floor_ready, img + 1)
                act.activation(std, var_floor, ACT.Sqrt, bias=eps[:, 0:1]).then_inc(std_ready, 1)
                act.activation(bottom[:, 1, ROWS - 1, :], ident[:, 0:W], ACT.Identity, scale=0.0, bias=mean[:, 1:2])
                act.activation(bottom[CB:P, 2, ROWS - 1, :], ident[CB:P, 0:W], ACT.Identity, scale=0.0,
                               bias=mean[CB:P, 2:3]).then_inc(bottom_pads_ready, 1)

            def scale_weights_to_a(img):
                act.wait_ge(rstd_ready, img + 1)
                wait_past(act, m1_ready, img * SUBS)
                act.activation(wts[:, 0:CA], w_raw[:, 0:CA], ACT.Identity, scale=rstd[:, 0:1])
                act.activation(wts[:, C:C + WTS_BA], w_raw[:, C:C + WTS_BA], ACT.Identity,
                               scale=rstd[:, 1:2]).then_inc(weights_to_a_ready, 1)

            def scale_weights_to_b(img):
                wait_past(act, m2_ready[1], img * SUBS)
                act.activation(wts[:, CA:C], w_raw[:, CA:C], ACT.Identity, scale=rstd[:, 0:1])
                act.activation(wts[:, C + WTS_BA:WTS], w_raw[:, C + WTS_BA:WTS], ACT.Identity,
                               scale=rstd[:, 1:2]).then_inc(weights_to_b_ready, 1)

            def carry(img, s):
                act.wait_ge(s_ready, img * SUBS + s + 1)
                act.activation(q[:, :, 0, :], q[:, :, SUB_ROWS, :], ACT.Identity).then_inc(q_carried, 1)

            def evacuate(img, s, h):
                act.wait_ge(m2_ready[h], img * SUBS + s + 1)
                if s == 0 and h == 0:
                    act.wait_ge(bias_ready, img + 1)
                dst = rows(img, s, h * TILE_ROWS, TILE_ROWS)[:, 2, :, :].rearrange("p r c -> p (r c)")
                act.activation(dst, m2[:, h, :], ACT.Identity, bias=bias[:, 1:2]).then_inc(m2_evacuated[h], 1)

            stats_at = ((0, 1, 3), (0, 1, 3), (0, 1, 3), (0, 1, 2), (0, 1, 3), (1, 2, 2), (0, 0, 0), (0, 0, 0))
            assert sum(sum(counts) for counts in stats_at) == STATS and len(stats_at) == SUBS

            def next_statistics(img, s, place):
                first = sum(sum(counts) for counts in stats_at[:s]) + sum(stats_at[s][:place])
                statistics(img + 1, first, stats_at[s][place])

            def image(img, last=False):
                for s in range(SUBS):
                    if s < CARRIES - 1:
                        carry(img, s + 1)
                    elif s == SUBS - 1 and not last:
                        carry(img + 1, 0)
                        scale_weights_to_a(img + 1)
                    if not last:
                        next_statistics(img, s, 0)
                    evacuate(img, s, 0)
                    if not last:
                        next_statistics(img, s, 1)
                        if s == SUBS - 2:
                            mean_pads_and_std(img + 1)
                    evacuate(img, s, 1)
                    if not last:
                        next_statistics(img, s, 2)
                if not last:
                    scale_weights_to_b(img + 1)

            act.wait_ge(constants_ready, 1)
            act.wait_ge(consts_loaded, 64)
            statistics(0, 0, STATS // 2, kinds=(1,))
            mean_pads_and_std(0)
            carry(0, 0)
            scale_weights_to_a(0)
            scale_weights_to_b(0)
            image(0)
            with act.Fori(1, B - 1) as img:
                image(img)
            image(B - 1, last=True)

        @block.vector
        def _(dve):
            def sum_partials(img):
                dve.wait_ge(partial_ready, img * STATS + STATS // 2)
                dve.tensor_reduce(sums[:, :, 0], partials[:, :, 0:2, :].rearrange("p s t k -> p s (t k)"),
                                  AX.X, ALU.add)
                dve.tensor_reduce(sums[:, :, 1], partials[:, :, 2, :], AX.X, ALU.add).then_inc(sums_ready, 1)

            def reciprocal(img):
                dve.wait_ge(std_ready, img + 1)
                dve.reciprocal(rstd0, std).then_inc(rstd0_ready, 1)

            def total_bias(img):
                dve.wait_ge(bias_sums_ready, img + 1)
                wait_past(dve, m2_evacuated[1], img * SUBS)
                wait_past(dve, m1_evacuated, img * SUBS)
                dve.tensor_tensor(bias[:, :], bias_raw[:, :], bias_sums, ALU.subtract).then_inc(bias_ready, 1)

            part_a, part_b = slice(0, 2), slice(2, 3)

            def neighbours_inside(img, s):
                if s % 2 == 0:
                    k = s // 2
                    dve.wait_ge(loaded[k], landed(img, k))
                if s == SUBS - 1:
                    dve.wait_ge(bottom_pads_ready, img + 1)
                if s > 0:
                    dve.wait_ge(q_carried, CARRIES * img + s)
                else:
                    wait_past(dve, s_ready, img * SUBS)
                x9 = rows(img, s, 0, SUB_ROWS + 1)
                for t, ready in ((part_a, q_inside_a_ready), (part_b, q_inside_b_ready)):
                    dve.tensor_tensor(q[:, t, 1:SUB_ROWS + 1, 1:W], x9[:, t, 0:SUB_ROWS, 1:W],
                                      x9[:, t, 1:SUB_ROWS + 1, 0:W - 1], ALU.add).then_inc(ready, 1)

            def neighbour_sum(img, s):
                g = img * SUBS + s
                dve.wait_ge(q_edges_ready, g + 1)
                wait_past(dve, m2_ready[1], g - 1)
                zs = z[:, s % 2, :, :].rearrange("p t (r c) -> p t r c", c=W)
                for t, inside_ready, ready in ((part_a, q_inside_a_ready, s_a_ready),
                                               (part_b, q_inside_b_ready, s_ready)):
                    dve.wait_ge(inside_ready, g + 1)
                    dve.tensor_tensor(zs[:, t, :, :], q[:, t, 0:SUB_ROWS, 0:W], q[:, t, 1:SUB_ROWS + 1, 1:QW],
                                      ALU.add).then_inc(ready, 1)

            def stencil(img, s):
                here = rows(img, s, 0, SUB_ROWS).rearrange("p t r c -> p t (r c)")
                for t, ready in ((part_a, s_a_ready), (part_b, s_ready)):
                    dve.wait_ge(ready, img * SUBS + s + 1)
                    zs = z[:, s % 2, t, :]
                    op = dve.scalar_tensor_tensor(out=zs, in0=here[:, t, :], scalar=5.0, in1=zs,
                                                  op0=ALU.mult, op1=ALU.subtract)
                op.then_inc(z_ready, 1)

            def evacuate(img, s):
                dve.wait_ge(m1_ready, img * SUBS + s + 1)
                if s == 0:
                    dve.wait_ge(bias_ready, img + 1)
                dst = rows(img, s, 0, SUB_ROWS)[:, 0:2, :, :].rearrange("p t r c -> p t (r c)")
                dve.scalar_tensor_tensor(out=dst, in0=m1[:, :, :, :].rearrange("p t h c -> p t (h c)"),
                                         scalar=bias[:, 0:1], in1=dst,
                                         op0=ALU.add, op1=ALU.add).then_inc(m1_evacuated, 1)

            def image(img, last=False):
                for s in range(SUBS):
                    if s < SUBS - 1:
                        neighbours_inside(img, s + 1)
                        neighbour_sum(img, s + 1)
                        if s == 0:
                            total_bias(img)
                        stencil(img, s + 1)
                        if s == SUBS - 2 and not last:
                            sum_partials(img + 1)
                        evacuate(img, s)
                    elif last:
                        evacuate(img, s)
                    else:
                        neighbours_inside(img + 1, 0)
                        neighbour_sum(img + 1, 0)
                        reciprocal(img + 1)
                        stencil(img + 1, 0)
                        evacuate(img, s)

            def first_sums(k, t):
                dve.tensor_reduce(partials[:, 0, t, k], slot(0, k)[:, t, 1:1 + SLOT_ROWS, :].rearrange(
                    "p t r c -> p t (r c)"), AX.X, ALU.add).then_inc(first_sums_ready, 1)

            for k in range(STEPS - 1):
                dve.wait_ge(loaded[k], landed(0, k))
                first_sums(k, slice(0, STREAMS))
                if k == 1:
                    neighbours_inside(0, 0)
            for t in range(2):
                dve.wait_ge(first_loaded[t], 16)
                first_sums(STEPS - 1, slice(t, t + 1))
            dve.wait_ge(loaded[STEPS - 1], landed(0, STEPS - 1))
            first_sums(STEPS - 1, slice(2, STREAMS))
            dve.wait_ge(first_sums_ready, STEPS + 2)
            sum_partials(0)
            neighbour_sum(0, 0)
            reciprocal(0)
            stencil(0, 0)
            dve.wait_ge(consts_loaded, 64)
            image(0)
            with dve.Fori(1, B - 1) as img:
                image(img)
            image(B - 1, last=True)

        @block.tensor
        def _(pe):
            w_aa, w_ab = wts[:, 0:CA], wts[:, CA:C]
            w_ba = wts[:, WTS_A:WTS_A + WTS_BA]
            w_bb = wts[:, WTS_A + WTS_BA:WTS]

            def group_averages(img):
                pe.wait_ge(sums_ready, img + 1)
                wait_past(pe, bias_ready, img)
                a, b = sums[:, :, 0], sums[:, :, 1]
                ba = GAVG_AA + GAVG_BB
                ab = ba + GAVG_BA
                low = P - GAVG_BA
                pe.matmul(group_stats[0:low, 0, :], gavg[:, 0:low], a, start=True, stop=True)
                pe.matmul(group_stats[low:P, 0, :], gavg[:, low:GAVG_AA], a, start=True, stop=False)
                pe.matmul(group_stats[low:P, 0, :], gavg[:, ba:ab], b, start=False, stop=True)
                pe.matmul(group_stats[:, 1, :], gavg[:, GAVG_AA:ba], b, start=True, stop=False)
                pe.matmul(group_stats[0:CB, 1, :], gavg[:, ab:GAVG], a, start=False, stop=True)
                pe.matmul(group_stats[CB:P, 1, :], gavg[:, ab:GAVG], a, start=False,
                          stop=True).then_inc(group_stats_ready, 1)

            def mean_through_weights(img):
                pe.wait_ge(mean_rstd_ready, img + 1)
                m_a, m_b = mean_rstd[:, 0:1], mean_rstd[:, 1:2]
                pe.matmul(bias_sums[:, 0:1], w_raw[:, 0:CA], m_a, start=True, stop=False)
                pe.matmul(bias_sums[:, 0:1], w_raw[0:CB, WTS_A:WTS_A + WTS_BA], m_b[0:CB, :], start=False, stop=True)
                pe.matmul(bias_sums[:, 1:2], w_raw[:, WTS_A + WTS_BA:WTS], m_b, start=True, stop=False)
                pe.matmul(bias_sums[0:CB, 1:2], w_raw[:, CA:C], m_a, start=False, stop=True)
                pe.matmul(bias_sums[CB:P, 1:2], w_raw[:, CA:C], m_a, start=False,
                          stop=True).then_inc(bias_sums_ready, 1)

            def mix_to_a(img, s, h):
                zt = z[:, s % 2, :, h * TILE:(h + 1) * TILE]
                if h == 0:
                    wait_past(pe, m1_evacuated, img * SUBS + s)
                if s == 0 and h == 0:
                    pe.wait_ge(weights_to_a_ready, img + 1)
                pe.matmul(m1[:, 0, h, :], w_aa, zt[:, 0, :], start=True, stop=False)
                pe.matmul(m1[:, 1, h, :], w_aa, zt[:, 1, :], start=True, stop=False)
                pe.matmul(m1[:, 0, h, :], w_ba[0:CB, :], zt[0:CB, 2, :], start=False, stop=True)
                mm = pe.matmul(m1[:, 1, h, :], w_ba[CB:P, :], zt[CB:P, 2, :], start=False, stop=True)
                if h == 1:
                    mm.then_inc(m1_ready, 1)

            def mix_to_b(img, s, h):
                zt = z[:, s % 2, :, h * TILE:(h + 1) * TILE]
                xt = rows(img, s, h * TILE_ROWS, TILE_ROWS)[:, 2, :, :].rearrange("p r c -> p (r c)")
                wait_past(pe, m2_evacuated[h], img * SUBS + s)
                if s == 0 and h == 0:
                    pe.wait_ge(weights_to_b_ready, img + 1)
                pe.matmul(m2[:, h, :], w_bb, zt[:, 2, :], start=True, stop=False)
                pe.matmul(m2[:, h, :], ident[:, :], xt, start=False, stop=False)
                pe.matmul(m2[0:CB, h, :], w_ab, zt[:, 0, :], start=False, stop=True)
                pe.matmul(m2[CB:P, h, :], w_ab, zt[:, 1, :], start=False, stop=True).then_inc(m2_ready[h], 1)

            def image(img, last=False):
                for s in range(SUBS):
                    if s == 0:
                        mean_through_weights(img)
                    pe.wait_ge(z_ready, img * SUBS + s + 1)
                    mix_to_a(img, s, 0)
                    mix_to_a(img, s, 1)
                    mix_to_b(img, s, 0)
                    if s == SUBS - 2 and not last:
                        group_averages(img + 1)
                    mix_to_b(img, s, 1)

            pe.wait_ge(consts_loaded, 64)
            group_averages(0)
            image(0)
            with pe.Fori(1, B - 1) as img:
                image(img)
            image(B - 1, last=True)


def group_average_matrices():
    a = np.arange(CA)
    b = CA + np.arange(P) % CB
    share = np.float32(1.0 / (GROUP_CHANNELS * H * W))
    same = [(k[:, None] // GROUP_CHANNELS == m[None, :] // GROUP_CHANNELS)
            for k, m in ((a, a), (b, b), (b, a[P - GAVG_BA:]), (a, b[:GAVG_AB]))]
    return np.where(np.concatenate(same, axis=1), share, np.float32(0.0))


def kernel(x, L0_conv_merge_w, L0_conv_merge_b):
    import concourse.bacc as bacc
    from concourse.bass_utils import run_bass_kernel_spmd

    x = np.ascontiguousarray(x)
    w = np.asarray(L0_conv_merge_w).reshape(C, C).T
    b = np.asarray(L0_conv_merge_b)
    w_lhst = np.zeros((P, WTS), w.dtype)
    w_lhst[:, 0:C] = w[0:CA, :]
    for half in range(2):
        part = slice(half * CB, (half + 1) * CB)
        w_lhst[part, WTS_A:WTS_A + WTS_BA] = w[CA:C, 0:CA]
        w_lhst[part, WTS_A + WTS_BA + half * CB:WTS_A + WTS_BA + (half + 1) * CB] = w[CA:C, CA:C]
    bias_cols = np.stack([b[0:CA], np.concatenate([b[CA:C], b[CA:C]])], axis=1)

    nc = bacc.Bacc("TRN2", target_bir_lowering=False, num_devices=1)
    arrays = {
        "x_dram": x,
        "w_lhst_dram": w_lhst,
        "bias_cols_dram": np.ascontiguousarray(bias_cols),
        "group_avg_dram": np.ascontiguousarray(group_average_matrices()),
        "identity_dram": np.eye(P, dtype=np.float32),
    }
    args = [nc.dram_tensor(n, a.shape, mybir.dt.from_np(a.dtype), kind="ExternalInput").ap()
            for n, a in arrays.items()]
    args.append(nc.dram_tensor("out_dram", (B, C, H, W), F32, kind="ExternalOutput").ap())
    conv_preact_kernel(nc, *args)
    r = run_bass_kernel_spmd(nc, [arrays], core_ids=[0])
    return r.results[0]["out_dram"]
```
